# Optimizing a Trainium2 kernel written in Bass

```python
import numpy as np
import jax
import jax.numpy as jnp

def _softmax(x, axis=-1):
    return jax.nn.softmax(x, axis=axis)

def _gelu(x):
    return jax.nn.gelu(x, approximate=True)

def _silu(x):
    return jax.nn.silu(x)

def _sigmoid(x):
    return jax.nn.sigmoid(x)

def _layernorm(x, axis=-1, eps=1e-05):
    m = jnp.mean(x, axis=axis, keepdims=True)
    v = jnp.var(x, axis=axis, keepdims=True)
    return (x - m) / jnp.sqrt(v + eps)

def _scatter_add(tgt, idx, src, axis=0):
    return tgt.at[idx].add(src)

def _segment_sum(src, seg, n):
    return jax.ops.segment_sum(src, seg, n)
kernel_name = 'mk_adj_resnorm_d2_adj_r2_6adcec'

def setup_inputs(seed: int=0):
    np.random.seed(seed)
    _w = jnp.asarray

    def _rec_inputs():
        import jax
        import jax.numpy as jnp
        _gk = jax.random.key(seed)
        x = -0.0002928 + 1 * jax.random.normal(jax.random.fold_in(_gk, 1), (8192, 128), jnp.float32)
        _a = jax.random.bernoulli(jax.random.fold_in(_gk, 2), 0.000488281, (8192, 8192))
        _a = jnp.logical_or(_a, jnp.eye(8192, dtype=bool))
        _af = _a.astype(jnp.float32)
        _af = _af * jax.random.uniform(jax.random.fold_in(_gk, 3), (8192, 8192), jnp.float32, 0.05, 6.10351e-05)
        adj = _af
        return (x, adj)
    x, adj = _rec_inputs()

    def _L0_gnn_setup():
        import jax, jax.numpy as jnp
        import numpy as np
        N_NODES = 8192
        D_FEAT = 128
        key = jax.random.key(seed)
        k1, k2, k3, k4 = jax.random.split(key, 4)
        X = jax.random.normal(k1, (N_NODES, D_FEAT), dtype=jnp.float32)
        A_hat = jax.random.uniform(k2, (N_NODES, N_NODES), dtype=jnp.float32) / N_NODES
        w = jax.random.uniform(k3, (N_NODES,), dtype=jnp.float32)
        W_agg = jax.random.normal(k4, (D_FEAT, D_FEAT), dtype=jnp.float32) / np.sqrt(D_FEAT)
        return {'X': X, 'A_hat': A_hat, 'w': w, 'W_agg': W_agg}
    _L0_gnn_all = _L0_gnn_setup()
    _L0_gnn_in = {k: v for k, v in _L0_gnn_all.items() if k in ('w', 'W_agg')}
    del _L0_gnn_all

    def _L1_gnn_setup():
        import jax, jax.numpy as jnp
        import numpy as np
        N = 8192
        F_IN = 128
        F_OUT = 128
        EPS = 0.0001
        key = jax.random.key(seed)
        k1, k2, k3 = jax.random.split(key, 3)
        features = jax.random.normal(k1, (N, F_IN), dtype=jnp.float32)
        adj = jax.random.uniform(k2, (N, N), dtype=jnp.float32)
        limit = float(np.sqrt(6.0 / (F_IN + F_OUT)))
        weight = jax.random.uniform(k3, (F_IN, F_OUT), dtype=jnp.float32, minval=-limit, maxval=limit)
        return {'features': features, 'adj': adj, 'weight': weight}
    _L1_gnn_all = _L1_gnn_setup()
    _L1_gnn_in = {k: v for k, v in _L1_gnn_all.items() if k in ('weight',)}
    del _L1_gnn_all
    return {'x': x, 'adj': adj, 'L0_gnn_w': _L0_gnn_in['w'], 'L0_gnn_W_agg': _L0_gnn_in['W_agg'], 'L1_gnn_weight': _L1_gnn_in['weight']}

def reference(x, adj, L0_gnn_w, L0_gnn_W_agg, L1_gnn_weight):
    import jax
    import jax.numpy as jnp

    def _L0_gnn_ref(X, A_hat, w, W_agg):
        import jax, jax.numpy as jnp
        import numpy as np
        N_NODES = 8192
        D_FEAT = 128
        agg = jnp.matmul(jnp.matmul(A_hat, X), W_agg)
        agg = jax.nn.relu(agg)
        s = jax.nn.sigmoid(w)[:, None]
        return s * agg + (1.0 - s) * X

    def _L1_gnn_ref(features, adj, weight):
        import jax, jax.numpy as jnp
        import numpy as np
        N = 8192
        F_IN = 128
        F_OUT = 128
        EPS = 0.0001
        support = jnp.matmul(features, weight)
        adj_norm = adj / jnp.sum(adj, axis=1, keepdims=True)
        out = jax.nn.relu(jnp.matmul(adj_norm, support)) + EPS
        return out
    x = _layernorm(x + _L0_gnn_ref(x, adj, L0_gnn_w, L0_gnn_W_agg), axis=-1)
    x = _layernorm(x + _L1_gnn_ref(x, adj, L1_gnn_weight), axis=-1)
    return x

_drawn_inputs = setup_inputs


def setup_inputs(seed=0):
    import zlib

    import numpy as np

    out = dict(_drawn_inputs(seed))
    spreads = {}
    factors = {}
    for name, (base, spread) in spreads.items():
        noise = np.random.default_rng([zlib.crc32(name.encode()), seed]).standard_normal(out[name].shape)
        drawn = base * np.exp(spread * noise) if base else spread * noise
        out[name] = jnp.asarray(drawn.astype(out[name].dtype))
    for name, factor in factors.items():
        out[name] = (out[name] * factor).astype(out[name].dtype)
    return out
```

```python
import numpy as np
import concourse.bass as bass
from concourse import mybir
from contextlib import ExitStack

F32 = mybir.dt.float32
F32R = mybir.dt.float32r
ALU = mybir.AluOpType
ACT = mybir.ActivationFunctionType
AX = mybir.AxisListType

P = 128
N = 8192
D = 128
ROWS = 512
SUB = ROWS // P
NROW = N // ROWS
KU = 2
UCOLS = KU * P
NU = 4
SCOLS = NU * UCOLS
NSB = N // SCOLS
KT = N // P
RB = SCOLS // ROWS
XT = 8
TSLOTS = 2
LN_EPS = 1e-5
OUT_EPS = 1e-4


def build(nc, x, adj, w, w_agg, weight, out):
    assert NROW * ROWS == N and NSB * SCOLS == N and SCOLS == 2 * ROWS and NROW % 4 == 0
    n_pass1 = NROW * NSB
    partial = nc.dram_tensor("partial", (NROW, P, ROWS), F32, kind="Internal").ap()

    a_units = adj.rearrange("(r s p) (c k) -> r c p s k", s=SUB, p=P, k=UCOLS)
    x_tiles = x.rearrange("(t p) d -> p t d", p=P)
    out_tiles = out.rearrange("(r s p) d -> r p s d", s=SUB, p=P)
    w_rows = w.rearrange("(t p) -> t p", p=P)

    with ExitStack() as ctx:
        def sb(name, shape, dt=F32):
            return ctx.enter_context(nc.sbuf_tensor(name, shape, dt))

        def ps(name, shape):
            return ctx.enter_context(nc.psum_tensor(name, shape, F32))

        def sem(name):
            return ctx.enter_context(nc.semaphore(name))

        x_hi = sb("x_hi", [P, KT, D], F32R)
        x_lo = sb("x_lo", [P, KT, D], F32R)
        z_hi = sb("z_hi", [P, KT, D], F32R)
        z_lo = sb("z_lo", [P, KT, D], F32R)
        x1_last = sb("x1_last", [P, KT])
        raw = sb("raw", [P, NU, SUB, UCOLS])
        a_hi = sb("a_hi", [P, NU, KU, ROWS], F32R)
        a_lo = sb("a_lo", [P, NU, KU, ROWS], F32R)
        ident = sb("ident", [P, P])
        zeros = sb("zeros", [P, ROWS], F32R)
        w0 = sb("w0", [P, D])
        w1 = sb("w1", [P, D])
        w1_row = sb("w1_row", [P, D])
        w_in = sb("w_in", [KT, P])
        exp_w = sb("exp_w", [P, KT])
        gate = sb("gate", [P, SUB + KT])
        keep = sb("keep", [P, KT])
        minus_half = sb("minus_half", [P, SUB])
        x_in = sb("x_in", [P, 2, XT, D])
        agg = sb("agg", [P, ROWS])
        part_out = sb("part_out", [P, ROWS])
        part_in = sb("part_in", [P, ROWS])
        act_out = sb("act_out", [P, SUB, D])
        inv_sum = sb("inv_sum", [P, SUB])
        v = sb("v", [P, SUB, D])
        sq = sb("sq", [P, SUB, D])
        fold = sb("fold", [P, SUB, D // 2])
        y = sb("y", [P, SUB, D])
        mean = sb("mean", [P, SUB])
        var = sb("var", [P, SUB])
        rstd = sb("rstd", [P, SUB])

        turned = ps("turned", [P, TSLOTS, KU, ROWS])
        acc = ps("acc", [P, 2, ROWS])
        acc_z = ps("acc_z", [P, ROWS])
        sums = acc_z[:, 0:SUB]
        w_cols = acc_z[:, 0:KT]
        dense = ps("dense", [P, SUB, D])

        raw_loaded = [sem(f"raw_loaded{u}") for u in range(NU)]
        turn_done = sem("turn_done")
        hi_done = sem("hi_done")
        lo_done = sem("lo_done")
        mul_done = sem("mul_done")
        x_loaded = [sem(f"x_loaded{b}") for b in range(2)]
        x_ready = sem("x_ready")
        w_loaded = sem("w_loaded")
        weights_loaded = sem("weights_loaded")
        ident_ready = sem("ident_ready")
        zeros_ready = sem("zeros_ready")
        w_turned = sem("w_turned")
        exp_done = sem("exp_done")
        gate_step = sem("gate_step")
        pool_step = sem("pool_step")
        agg_ready = sem("agg_ready")
        part_ready = sem("part_ready")
        part_stored = sem("part_stored")
        part_loaded = sem("part_loaded")
        dense_done = sem("dense_done")
        inv_done = sem("inv_done")
        act_done = sem("act_done")
        row_out = sem("row_out")
        y_stored = sem("y_stored")

        def at1(r, c):
            return r * NSB + (NSB - 1) - c

        def at2(a, b, second, c):
            if second:
                return start2(a, b, True) + (NSB - 1 - c)
            return a * (2 * (NSB + 1) - 1) + b * (NSB + 1) + c + n_pass1

        def start2(a, b, second):
            if second:
                return a * (2 * (NSB + 1) - 1) + b * (NSB + 1) + (n_pass1 + NSB)
            return a * (2 * (NSB + 1)) + b * (NSB + 1) + n_pass1

        def multiplied_before(n):
            return n * NU + NU

        block = ctx.enter_context(nc.Block())

        @block.sync
        def _(sp):
            def load(n, r, c):
                for u in range(NU):
                    sp.wait_ge(turn_done, n * NU + (u + 1))
                    sp.dma_start(raw[:, u], a_units[r, c * NU + u]).then_inc(raw_loaded[u], 16)

            with sp.Fori(0, NROW) as r:
                with sp.Fori(0, NSB) as k:
                    load(r * NSB + k, r, k * -1 + (NSB - 1))
            with sp.Fori(0, NROW // 4) as a:
                with sp.Fori(0, 2) as b:
                    with sp.Fori(a, NSB) as c:
                        load(at2(a, b, False, c), a * 2 + b, c)
                    with sp.Fori(0, a + 1) as j:
                        load(start2(a, b, True) + j, a * -2 + b * -1 + (NROW - 1),
                             j * -1 + (NSB - 1))

        @block.tensor
        def _(pe):
            def turn(n, u):
                slot = u % TSLOTS
                pe.wait_ge(raw_loaded[u], n * 16 + 16)
                for kk in range(KU):
                    for s in range(SUB):
                        last = nc.tensor.transpose(turned[:, slot, kk, s * P:(s + 1) * P],
                                                   raw[:, u, s, kk * P:(kk + 1) * P], ident[:, :])
                last.then_inc(turn_done, 1)

            def product(dst, left, right, start=False, stop=False):
                return nc.tensor.matmul(dst, left, right, start=start, stop=stop,
                                        skip_group_check=True)

            def turn_ahead(n, u):
                pe.wait_ge(lo_done, n * NU + (u + 1))
                ahead = u + TSLOTS
                turn(n + ahead // NU, ahead % NU)

            def multiply(n, u, c, dst, hi, lo, start, stop, z_too=None, ahead_if=None):
                tiles = [(c * NU + u) * KU + kk for kk in range(KU)]
                pe.wait_ge(hi_done, n * NU + (u + 1))
                for kk, t in enumerate(tiles):
                    product(dst, lo[:, t, :], a_hi[:, u, kk, :], start=start and kk == 0)
                    product(dst, hi[:, t, :], a_hi[:, u, kk, :])
                if ahead_if is None:
                    turn_ahead(n, u)
                else:
                    pe.wait_ge(lo_done, n * NU + (u + 1))
                    with pe.If(ahead_if):
                        turn_ahead(n, u)
                if z_too is not None:
                    with pe.If(z_too):
                        for kk, t in enumerate(tiles):
                            product(acc_z[:, :], z_lo[:, t, :], a_hi[:, u, kk, :])
                            product(acc_z[:, :], z_hi[:, t, :], a_hi[:, u, kk, :])
                            product(acc_z[:, :], z_hi[:, t, :], a_lo[:, u, kk, :])
                for kk, t in enumerate(tiles):
                    last = product(dst, hi[:, t, :], a_lo[:, u, kk, :], stop=stop and kk == KU - 1)
                last.then_inc(mul_done, 1)

            def dense_layer(count, weights):
                pe.wait_ge(agg_ready, count + 2)
                pe.wait_ge(act_done, count)
                for s in range(SUB):
                    last = nc.tensor.matmul(dense[:, s, :], agg[:, s * P:(s + 1) * P], weights[:, :],
                                            start=True, stop=True)
                return last

            def row_sums(count):
                pe.wait_ge(agg_ready, count + 2)
                for s in range(SUB):
                    nc.tensor.matmul(sums[:, s:s + 1], agg[:, s * P:(s + 1) * P],
                                     ident[:, D - 1:D], start=True, stop=True)

            pe.sem_inc(turn_done, NU)
            pe.sem_inc(mul_done, NU)
            pe.sem_inc(agg_ready, 2)
            pe.sem_inc(act_done, 1)
            pe.sem_inc(row_out, 1)
            pe.wait_ge(ident_ready, 1)
            pe.wait_ge(w_loaded, 16)
            nc.tensor.transpose(w_cols, w_in[:, :], ident[0:KT, 0:KT]).then_inc(w_turned, 1)
            pe.wait_ge(zeros_ready, 1)
            pe.wait_ge(weights_loaded, 48)
            for u in range(TSLOTS):
                turn(0, u)

            with pe.Fori(0, NROW // 2) as a:
                for b in range(2):
                    r = a * 2 + b
                    for c in reversed(range(NSB)):
                        n = at1(r, c)
                        if c == NSB - 2:
                            pe.wait_ge(exp_done, 1)
                            pe.wait_ge(part_ready, r)
                            nc.tensor.matmul(acc_z[:, :], zeros[:, 0:P], zeros[:, :],
                                             start=True, stop=True)
                        pe.wait_ge(x_ready, NSB - c)
                        if c < NSB - 1:
                            with pe.If(c < a):
                                pe.wait_ge(row_out, 2 * c + 3)
                        for u in range(NU):
                            first, last = c == NSB - 1 and u == 0, c == 0 and u == NU - 1
                            if first:
                                pe.wait_ge(agg_ready, r + 1)
                            multiply(n, u, c, acc[:, b, :], x_hi, x_lo, first, last,
                                     z_too=(c < a) if c < NSB - 1 else None)
                            if c == NSB - 1 and u == 1:
                                if b == 0:
                                    with pe.If(a > 0):
                                        dense_layer(r, w0).then_inc(dense_done, 1)
                                else:
                                    dense_layer(r, w0).then_inc(dense_done, 1)
            dense_layer(NROW, w0).then_inc(dense_done, 1)

            def finish2(count):
                row_sums(count)
                dense_layer(count, w1).then_inc(dense_done, 1)

            def block2(a, b, second):
                before = a * 4 + b * 2 + (NROW + second)
                for c in reversed(range(NSB)) if second else range(NSB):
                    n = at2(a, b, second, c)

                    def superblock():
                        pe.wait_ge(row_out, min(2 * c + 3, NROW + 1))
                        for u in range(NU):
                            end = second and c == NSB - NROW // 4 and u >= NU - TSLOTS
                            multiply(n, u, c, acc[:, second, :], z_hi, z_lo, False,
                                     False,
                                     ahead_if=(a * 2 + b < NROW // 2 - 1) if end else None)
                            if c == NSB - 1 and u == TSLOTS - 1:
                                if second:
                                    finish2(before)
                                else:
                                    with pe.If(a * 2 + b > 0):
                                        finish2(before)
                    if c == NSB - 1:
                        superblock()
                    else:
                        with pe.If(c >= a if not second else c + a >= NSB - 1):
                            superblock()

            with pe.Fori(0, NROW // 4) as a:
                with pe.Fori(0, 2) as b:
                    for second in (0, 1):
                        done = a * 4 + b * 2 + (NROW + second)
                        pe.wait_ge(agg_ready, done + 1)
                        nc.tensor.matmul(acc[:, second, :], zeros[:, 0:P], zeros[:, :],
                                         start=True, stop=True)
                        block2(a, b, second)
            finish2(2 * NROW)

        @block.scalar
        def _(act):
            act.dma_start(w_in[:, :], w_rows).then_inc(w_loaded, 16)
            act.dma_start(w0[:, :], w_agg).then_inc(weights_loaded, 16)
            act.dma_start(w1[:, :], weight).then_inc(weights_loaded, 16)
            act.dma_start(w1_row[:, :], weight[D - 1:D, :].to_broadcast([P, D])
                          ).then_inc(weights_loaded, 16)
            act.wait_ge(w_turned, 1)
            nc.scalar.activation(exp_w[:, :], w_cols, ACT.Exp, scale=-1.0).then_inc(exp_done, 1)

            def high(n, u):
                act.wait_ge(turn_done, n * NU + (u + 1 + NU))
                act.wait_ge(mul_done, n * NU + (u + 1))
                nc.scalar.activation(a_hi[:, u], turned[:, u % TSLOTS], ACT.Copy
                                     ).then_inc(hi_done, 1)

            def aggregate(nxt, b):
                act.wait_ge(mul_done, multiplied_before(nxt * NSB))
                nc.scalar.activation(agg[:, :], acc[:, b, :], ACT.Copy).then_inc(agg_ready, 1)

            def relu0(nxt):
                act.wait_ge(dense_done, nxt)
                act.wait_ge(row_out, nxt)
                act.wait_ge(gate_step, 3)
                for s in range(SUB):
                    last = nc.scalar.activation(act_out[:, s, :], dense[:, s, :], ACT.Relu,
                                                scale=gate[:, bass.ds(nxt * SUB + s, 1)])
                last.then_inc(act_done, 1)

            def relu1(n2):
                act.wait_ge(dense_done, n2 + NROW)
                act.wait_ge(inv_done, n2)
                act.wait_ge(row_out, n2 + NROW)
                for s in range(SUB):
                    last = nc.scalar.activation(act_out[:, s, :], dense[:, s, :], ACT.Relu,
                                                scale=inv_sum[:, s:s + 1])
                last.then_inc(act_done, 1)

            with act.Fori(0, NROW // 2) as a:
                for b in range(2):
                    r = a * 2 + b
                    for u in range(TSLOTS):
                        high(r * NSB, u)
                    if b:
                        aggregate(r, 0)
                    else:
                        with act.If(a > 0):
                            aggregate(r, 1)
                    for u in range(TSLOTS, NU):
                        high(r * NSB, u)
                    if b:
                        relu0(r)
                    else:
                        with act.If(a > 0):
                            relu0(r)
                    with act.Fori(1, NSB) as k:
                        for u in range(NU):
                            high(r * NSB + k, u)
            aggregate(NROW, 1)
            relu0(NROW)
            with act.Fori(0, NROW // 4) as a:
                with act.Fori(0, 2) as b:
                    for second in (0, 1):
                        before = a * 4 + b * 2 + second
                        left = a + 1 if second else NSB - a
                        with act.Fori(0, left) as j:
                            for u in range(NU):
                                high(start2(a, b, second) + j, u)
                            with act.If(j < 1 if second else j + 1 >= left):
                                if second:
                                    relu1(before)
                                else:
                                    with act.If(a * 2 + b > 0):
                                        relu1(before)
            relu1(NROW)

        @block.vector
        def _(dve):
            nc.vector.memset(zeros[:, :].bitcast(F32), 0.0).then_inc(zeros_ready, 1)
            dve.wait_ge(exp_done, 1)
            nc.vector.tensor_scalar(exp_w[:, :], exp_w[:, :], 1.0, None, ALU.add).then_inc(gate_step, 1)
            dve.wait_ge(gate_step, 1)
            nc.vector.reciprocal(gate[:, SUB:], exp_w[:, :]).then_inc(gate_step, 1)
            dve.wait_ge(gate_step, 2)
            nc.vector.tensor_scalar(keep[:, :], gate[:, SUB:], -1.0, 2.0, ALU.mult, ALU.add
                                    ).then_inc(gate_step, 1)

            def low(n, u):
                dve.wait_ge(hi_done, n * NU + (u + 1))
                nc.vector.tensor_tensor(a_lo[:, u], turned[:, u % TSLOTS],
                                        a_hi[:, u].bitcast(F32), ALU.subtract).then_inc(lo_done, 1)

            def save_part(nxt):
                dve.wait_ge(mul_done, multiplied_before(nxt * NSB))
                dve.wait_ge(row_out, nxt)
                nc.vector.tensor_copy(part_out[:, :], acc_z[:, :]).then_inc(part_ready, 1)

            with dve.Fori(0, NROW // 2) as a:
                for b in range(2):
                    r = a * 2 + b
                    for u in range(TSLOTS):
                        low(r * NSB, u)
                    if b:
                        save_part(r)
                    else:
                        with dve.If(a > 0):
                            save_part(r)
                    for u in range(TSLOTS, NU):
                        low(r * NSB, u)
                    with dve.Fori(1, NSB) as k:
                        for u in range(NU):
                            low(r * NSB + k, u)
            save_part(NROW)

            def aggregate(n2, nxt, which):
                dve.wait_ge(mul_done, multiplied_before(nxt))
                dve.wait_ge(part_loaded, n2 * 16)
                nc.vector.tensor_tensor(agg[:, :], acc[:, which, :], part_in[:, :],
                                        ALU.add).then_inc(agg_ready, 1)

            def inverse(n2):
                dve.wait_ge(dense_done, n2 + NROW)
                nc.vector.reciprocal(inv_sum[:, :], sums).then_inc(inv_done, 1)

            with dve.Fori(0, NROW // 4) as a:
                with dve.Fori(0, 2) as b:
                    for second in (0, 1):
                        before = a * 4 + b * 2 + second
                        left = a + 1 if second else NSB - a
                        begin = start2(a, b, second)
                        with dve.Fori(0, left) as j:
                            n = begin + j
                            for u in range(TSLOTS):
                                low(n, u)
                            with dve.If(j < 1 if second else j + 1 >= left):
                                if second:
                                    aggregate(before, begin, 0)
                                else:
                                    with dve.If(a * 2 + b > 0):
                                        aggregate(before, begin, 1)
                            for u in range(TSLOTS, NU):
                                low(n, u)
                            with dve.If(j < 1 if second else j + 1 >= left):
                                if second:
                                    inverse(before)
                                else:
                                    with dve.If(a * 2 + b > 0):
                                        inverse(before)
            aggregate(NROW, n_pass1 + NROW // 2 * (NSB + 1), 1)
            inverse(NROW)

        @block.gpsimd
        def _(pool):
            g = nc.gpsimd
            g.memset(ident[:, :], 0.0).then_inc(pool_step, 1)
            pool.wait_ge(pool_step, 1)
            g.affine_select(out=ident[:, :], in_=ident[:, :], compare_op=ALU.not_equal, fill=1.0,
                            base=0, pattern=[[-1, P]], channel_multiplier=1).then_inc(ident_ready, 1)
            g.memset(minus_half[:, :], -0.5).then_inc(pool_step, 1)
            for k in range(2):
                c = NSB - 1 - k
                pool.dma_start(x_in[:, k], x_tiles[:, c * XT:(c + 1) * XT, :]).then_inc(x_loaded[k], 16)
            for k in range(NSB):
                tiles = slice((NSB - 1 - k) * XT, (NSB - k) * XT)
                pool.wait_ge(x_loaded[k % 2], 16 * (k // 2) + 16)
                g.tensor_copy(x_hi[:, tiles, :], x_in[:, k % 2]).then_inc(pool_step, 1)
                pool.wait_ge(pool_step, 3 + k)
                g.tensor_tensor(x_lo[:, tiles, :], x_in[:, k % 2], x_hi[:, tiles, :].bitcast(F32),
                                ALU.subtract).then_inc(x_ready, 1)
                if k + 2 < NSB:
                    pool.wait_ge(x_ready, k + 1)
                    c = NSB - 3 - k
                    pool.dma_start(x_in[:, k % 2], x_tiles[:, c * XT:(c + 1) * XT, :]
                                   ).then_inc(x_loaded[k % 2], 16)
            pool.wait_ge(weights_loaded, 48)
            g.tensor_tensor(w1[:, :], w1[:, :], w1_row[:, :], ALU.subtract).then_inc(pool_step, 1)
            pool.wait_ge(gate_step, 3)
            pool.wait_ge(pool_step, NSB + 3)

            def wide(ap):
                return ap.unsqueeze(2).to_broadcast([P, SUB, D])

            def row_sum(step, dst, src):
                half = D // 2
                step(g.tensor_tensor(fold[:, :, 0:half], src[:, :, 0:half], src[:, :, half:D], ALU.add))
                while half > 2:
                    half //= 2
                    step(g.tensor_tensor(fold[:, :, 0:half], fold[:, :, 0:half],
                                         fold[:, :, half:2 * half], ALU.add))
                step(g.tensor_tensor(dst, fold[:, :, 0], fold[:, :, 1], ALU.add))

            def norm(step, dst):
                row_sum(step, mean[:, :], v)
                step(g.tensor_scalar(mean[:, :], mean[:, :], 1.0 / D, None, ALU.mult))
                step(g.tensor_tensor(v[:, :, :], v[:, :, :], wide(mean[:, :]), ALU.subtract))
                step(g.tensor_tensor(sq[:, :, :], v[:, :, :], v[:, :, :], ALU.mult))
                row_sum(step, var[:, :], sq)
                step(g.tensor_scalar(var[:, :], var[:, :], 1.0 / D, LN_EPS, ALU.mult, ALU.add))
                step(g.tensor_tensor(rstd[:, :], var[:, :], minus_half[:, :], ALU.pow))
                return g.tensor_tensor(dst, v[:, :, :], wide(rstd[:, :]), ALU.mult)

            def counter():
                pool.sem_clear(pool_step)
                count = [0]

                def step(ins):
                    count[0] += 1
                    ins.then_inc(pool_step, 1)
                    pool.wait_ge(pool_step, count[0])
                return step, count

            with pool.Fori(0, NROW) as r:
                step, count = counter()
                tiles = bass.ds(r * SUB, SUB)
                pool.wait_ge(part_ready, r + 1)
                pool.dma_start(partial[r], part_out[:, :]).then_inc(part_stored, 16)
                step(g.tensor_tensor(v[:, :, :], x_hi[:, tiles, :].bitcast(F32),
                                     x_lo[:, tiles, :].bitcast(F32), ALU.add))
                step(g.tensor_tensor(v[:, :, :], v[:, :, :], wide(keep[:, tiles]), ALU.mult))
                pool.wait_ge(act_done, r + 2)
                step(g.tensor_tensor(v[:, :, :], v[:, :, :], act_out[:, :, :], ALU.add))
                step(norm(step, y[:, :, :]))
                step(g.tensor_copy(x1_last[:, tiles], y[:, :, D - 1]))
                step(g.memset(y[:, :, D - 1:D], 1.0))
                step(g.tensor_copy(z_hi[:, tiles, :], y[:, :, :]))
                pool.wait_ge(part_stored, r * 16 + 16)
                g.tensor_tensor(z_lo[:, tiles, :], y[:, :, :], z_hi[:, tiles, :].bitcast(F32),
                                ALU.subtract).then_inc(row_out, 1)

            pool.wait_ge(part_stored, NROW * 16)
            with pool.Fori(0, NROW // 4) as a:
                with pool.Fori(0, 2) as b:
                    for second in (0, 1):
                        g2 = a * 4 + b * 2 + second
                        r = a * -2 + b * -1 + (NROW - 1) if second else a * 2 + b
                        tiles = bass.ds(r * SUB, SUB)
                        step, count = counter()
                        pool.wait_ge(agg_ready, g2 + (NROW + 2))
                        step(g.tensor_tensor(v[:, :, :], z_hi[:, tiles, :].bitcast(F32),
                                             z_lo[:, tiles, :].bitcast(F32), ALU.add))
                        pool.dma_start(part_in[:, :], partial[r]).then_inc(part_loaded, 16)
                        step(g.tensor_copy(v[:, :, D - 1], x1_last[:, tiles]))
                        pool.wait_ge(act_done, g2 + (NROW + 2))
                        step(g.tensor_scalar(sq[:, :, :], act_out[:, :, :], OUT_EPS, None, ALU.add))
                        step(g.tensor_tensor(v[:, :, :], v[:, :, :], sq[:, :, :], ALU.add))
                        pool.wait_ge(y_stored, g2 * 16)
                        step(norm(step, y[:, :, :]))
                        pool.sem_inc(row_out, 1)
                        pool.dma_start(out_tiles[r], y[:, :, :]).then_inc(y_stored, 16)
            pool.wait_ge(y_stored, NROW * 16)


_INS = ["x", "adj", "L0_gnn_w", "L0_gnn_W_agg", "L1_gnn_weight"]


def kernel(**inputs):
    import concourse.bacc as bacc
    from concourse.bass_utils import run_bass_kernel_spmd

    nc = bacc.Bacc("TRN2", target_bir_lowering=False, num_devices=1)
    arrays, args = {}, []
    for name in _INS:
        a = np.ascontiguousarray(inputs[name])
        arrays[name] = a
        args.append(nc.dram_tensor(name, a.shape, mybir.dt.from_np(a.dtype), kind="ExternalInput").ap())
    out = nc.dram_tensor("y_out", (N, D), F32, kind="ExternalOutput").ap()
    build(nc, *args, out)
    return run_bass_kernel_spmd(nc, [arrays], core_ids=[0]).results[0]["y_out"]
```

```python
import numpy as np
import concourse.bass as bass
from concourse import mybir
from contextlib import ExitStack

F32 = mybir.dt.float32
F32R = mybir.dt.float32r
ALU = mybir.AluOpType
ACT = mybir.ActivationFunctionType
AX = mybir.AxisListType

P = 128
N = 8192
D = 128
ROWS = 512
SUB = ROWS // P
NROW = N // ROWS
TILES = 4
Q = P // 4
HALF = ROWS // 2
GROUPS = HALF // Q
LCOLS = 2 * P
SCOLS = 2 * ROWS
NSB = N // SCOLS
KT = N // P
XT = SCOLS // P
PSLOTS = 2
LN_EPS = 1e-5
OUT_EPS = 1e-4


def build(nc, x, adj, w, w_agg, weight, out):
    assert NROW * ROWS == N and NSB * SCOLS == N and SCOLS == 2 * ROWS and NROW % 4 == 0
    n_pass1 = NROW * NSB
    partial = nc.dram_tensor("partial", (NROW, P, ROWS), F32, kind="Internal").ap()

    a_p = adj.rearrange("(r s p) (c k) -> r c p s k", s=SUB, p=P, k=LCOLS)
    a_d = adj.rearrange("(r g i) (q k) -> r q i g k", g=GROUPS, i=Q, k=P)
    x_rows = x.rearrange("(r t p) d -> r p t d", t=TILES, p=P)
    x_quarter = x.rearrange("(r q t i) d -> r q i t d", q=4, t=TILES, i=Q)
    out_rows = out.rearrange("(r t p) d -> r p t d", t=TILES, p=P)
    out_quarter = out.rearrange("(r q t i) d -> r q i t d", q=4, t=TILES, i=Q)
    w_rows = w.rearrange("(r t p) -> t r p", t=TILES, p=P)
    w_quarter = w.rearrange("(r q t i) -> t r q i", q=4, t=TILES, i=Q)

    with ExitStack() as ctx:
        def sb(name, shape, dt=F32):
            return ctx.enter_context(nc.sbuf_tensor(name, shape, dt))

        def ps(name, shape):
            return ctx.enter_context(nc.psum_tensor(name, shape, F32))

        def sem(name):
            return ctx.enter_context(nc.semaphore(name))

        x_hi = sb("x_hi", [P, KT, D], F32R)
        x_lo = sb("x_lo", [P, KT, D], F32R)
        z_hi = sb("z_hi", [P, KT, D], F32R)
        z_lo = sb("z_lo", [P, KT, D], F32R)
        x1_last = sb("x1_last", [P, KT])
        raw_p = sb("raw_p", [P, 2, SUB, LCOLS])
        raw_d = sb("raw_d", [P, 2, GROUPS, P])
        a_hi = sb("a_hi", [P, 2 * TILES, ROWS], F32R)
        a_lo = sb("a_lo", [P, 2 * TILES, ROWS], F32R)
        ident = sb("ident", [P, P])
        zeros = sb("zeros", [P, ROWS], F32R)
        w0 = sb("w0", [P, D])
        w1 = sb("w1", [P, D])
        w1_row = sb("w1_row", [P, D])
        w_in = sb("w_in", [KT, P])
        exp_w = sb("exp_w", [P, KT])
        gate = sb("gate", [P, SUB + KT])
        keep = sb("keep", [P, KT])
        minus_half = sb("minus_half", [P, SUB])
        x_in = sb("x_in", [P, 2, XT, D])
        agg = sb("agg", [P, ROWS])
        part_out = sb("part_out", [P, ROWS])
        part_in = sb("part_in", [P, ROWS])
        act_out = sb("act_out", [P, SUB, D])
        inv_sum = sb("inv_sum", [P, SUB])
        v = sb("v", [P, SUB, D])
        sq = sb("sq", [P, SUB, D])
        fold = sb("fold", [P, SUB, D // 2])
        y = sb("y", [P, SUB, D])
        mean = sb("mean", [P, SUB])
        var = sb("var", [P, SUB])
        rstd = sb("rstd", [P, SUB])

        turned_p = ps("turned_p", [P, PSLOTS, ROWS])
        turned_d = ps("turned_d", [P, TILES, HALF])
        acc = ps("acc", [P, 2, ROWS])
        acc_z = ps("acc_z", [P, ROWS])
        sums = acc_z[:, 0:SUB]
        w_cols = acc_z[:, 0:KT]
        dense = ps("dense", [P, SUB, D])

        p_loaded = [sem(f"p_loaded{v}") for v in range(2)]
        d_loaded = [sem(f"d_loaded{h}") for h in range(2)]
        p_turned = sem("p_turned")
        p_hi = sem("p_hi")
        p_lo = sem("p_lo")
        p_mul = sem("p_mul")
        d_turned = sem("d_turned")
        d_hi = sem("d_hi")
        d_lo = sem("d_lo")
        d_mul = sem("d_mul")
        x_loaded = [sem(f"x_loaded{b}") for b in range(2)]
        x_ready = sem("x_ready")
        w_loaded = sem("w_loaded")
        weights_loaded = sem("weights_loaded")
        ident_ready = sem("ident_ready")
        zeros_ready = sem("zeros_ready")
        w_turned = sem("w_turned")
        exp_done = sem("exp_done")
        gate_step = sem("gate_step")
        pool_step = sem("pool_step")
        agg_ready = sem("agg_ready")
        part_ready = sem("part_ready")
        part_stored = sem("part_stored")
        part_loaded = sem("part_loaded")
        dense_done = sem("dense_done")
        inv_done = sem("inv_done")
        act_done = sem("act_done")
        act_read = sem("act_read")
        row_out = sem("row_out")
        y_stored = sem("y_stored")

        def at1(r, c):
            return r * NSB + (NSB - 1) - c

        def at2(a, b, second, c):
            if second:
                return start2(a, b, True) + (NSB - 1 - c)
            return a * (2 * (NSB + 1) - 1) + b * (NSB + 1) + c + n_pass1

        def start2(a, b, second):
            if second:
                return a * (2 * (NSB + 1) - 1) + b * (NSB + 1) + (n_pass1 + NSB)
            return a * (2 * (NSB + 1)) + b * (NSB + 1) + n_pass1

        def multiplied_before(n):
            return n * 2 + 2

        def by_tile(ap, odd, tiled=False):
            if odd:
                return ap.rearrange("p (t q i) -> p t q i", t=TILES, q=4)
            order = "p (t q i) -> p q t i" if tiled else "p (q t i) -> p q t i"
            return ap.rearrange(order, t=TILES, q=4)

        block = ctx.enter_context(nc.Block())

        @block.sync
        def _(sp):
            def load(n, r, c):
                for h in range(2):
                    sp.wait_ge(d_turned, n * 2 + (h + 1))
                    for q in range(4):
                        sp.dma_start(raw_d[q * Q:(q + 1) * Q, h], a_d[r * 2 + h, c * XT + q]
                                     ).then_inc(d_loaded[h], 16)
                    sp.wait_ge(p_turned, n * TILES + 2 * (h + 1))
                    sp.dma_start(raw_p[:, h], a_p[r, c * (XT // 2) + (2 + h)]
                                 ).then_inc(p_loaded[h], 16)

            with sp.Fori(0, NROW) as r:
                with sp.Fori(0, NSB) as k:
                    load(r * NSB + k, r, k * -1 + (NSB - 1))
            with sp.Fori(0, NROW // 4) as a:
                for b in range(2):
                    with sp.Fori(a, NSB) as c:
                        load(at2(a, b, False, c), a * 2 + b, c)
                    with sp.Fori(0, a + 1) as j:
                        load(start2(a, b, True) + j, a * -2 + (NROW - 1 - b), j * -1 + (NSB - 1))

        @block.tensor
        def _(pe):
            def turn(n, j):
                pe.wait_ge(p_loaded[j // 2], n * 16 + 16)
                for s in range(SUB):
                    last = nc.tensor.transpose(
                        turned_p[:, j % PSLOTS, s * P:(s + 1) * P],
                        raw_p[:, j // 2, s, (j % 2) * P:(j % 2 + 1) * P], ident[:, :])
                last.then_inc(p_turned, 1)

            def product(dst, left, right, start=False):
                return nc.tensor.matmul(dst, left, right, start=start, stop=False,
                                        skip_group_check=True)

            def three(dst, hi, lo, t, at, start=False):
                product(dst, lo[:, t, :], a_hi[at], start=start)
                product(dst, hi[:, t, :], a_hi[at])
                return product(dst, hi[:, t, :], a_lo[at])

            def multiply_p(n, j, c, dst, hi, lo, start, z_too=None, ahead_if=None):
                t, at = c * XT + TILES + j, (slice(None), TILES + j, slice(None))
                pe.wait_ge(p_hi, n * TILES + (j + 1))
                product(dst, lo[:, t, :], a_hi[at], start=start)
                product(dst, hi[:, t, :], a_hi[at])
                pe.wait_ge(p_lo, n * TILES + (j + 1))
                ahead = j + PSLOTS
                if ahead_if is None:
                    turn(n + ahead // TILES, ahead % TILES)
                else:
                    with pe.If(ahead_if):
                        turn(n + ahead // TILES, ahead % TILES)
                if z_too is not None:
                    with pe.If(z_too):
                        three(acc_z[:, :], z_hi, z_lo, t, at)
                product(dst, hi[:, t, :], a_lo[at]).then_inc(p_mul, 1)

            def multiply_d(n, h, c, dst, hi, lo, z_too=None):
                rows = slice(h * HALF, (h + 1) * HALF)
                pe.wait_ge(d_lo, n * 2 + (h + 1))
                if z_too is not None:
                    with pe.If(z_too):
                        for t in range(TILES):
                            three(acc_z[:, rows], z_hi, z_lo, c * XT + t, (slice(None), t, rows))
                for t in range(TILES):
                    last = three(dst[:, rows], hi, lo, c * XT + t, (slice(None), t, rows))
                last.then_inc(d_mul, 1)

            def multiply(n, c, dst, hi, lo, start, z_too=None, ahead_if=None, between=None):
                for h in range(2):
                    for j in (2 * h, 2 * h + 1):
                        multiply_p(n, j, c, dst, hi, lo, start and j == 0, z_too,
                                   ahead_if if h else None)
                    multiply_d(n, h, c, dst, hi, lo, z_too)
                    if between and h == 0:
                        between()

            def dense_layer(count, weights):
                pe.wait_ge(agg_ready, count + 2)
                pe.wait_ge(act_done, count)
                for t in range(TILES):
                    last = nc.tensor.matmul(dense[:, t, :], agg_tile(t), weights[:, :],
                                            start=True, stop=True)
                return last

            def row_sums(count):
                pe.wait_ge(agg_ready, count + 2)
                for t in range(TILES):
                    nc.tensor.matmul(sums[:, t:t + 1], agg_tile(t), ident[:, D - 1:D],
                                     start=True, stop=True)

            def agg_tile(t):
                return agg[:, t * P:(t + 1) * P]

            pe.sem_inc(p_turned, TILES)
            pe.sem_inc(p_mul, TILES)
            pe.sem_inc(d_turned, 2)
            pe.sem_inc(d_mul, 2)
            pe.sem_inc(act_read, 1)
            pe.sem_inc(agg_ready, 2)
            pe.sem_inc(act_done, 1)
            pe.sem_inc(row_out, 1)
            pe.wait_ge(ident_ready, 1)
            pe.wait_ge(w_loaded, 16 * 2 * TILES)
            nc.tensor.transpose(w_cols, w_in[:, :], ident[0:KT, 0:KT]).then_inc(w_turned, 1)
            pe.wait_ge(zeros_ready, 1)
            pe.wait_ge(weights_loaded, 48)
            for j in range(PSLOTS):
                turn(0, j)

            with pe.Fori(0, NROW // 2) as a:
                for b in range(2):
                    r = a * 2 + b
                    for c in reversed(range(NSB)):
                        n = at1(r, c)
                        if c == NSB - 2:
                            pe.wait_ge(exp_done, 1)
                            pe.wait_ge(part_ready, r)
                            nc.tensor.matmul(acc_z[:, :], zeros[:, 0:P], zeros[:, :],
                                             start=True, stop=True)
                        pe.wait_ge(x_ready, NSB - c)
                        if c < NSB - 1:
                            with pe.If(c < a):
                                pe.wait_ge(row_out, 2 * c + 3)
                        first = c == NSB - 1
                        if first:
                            pe.wait_ge(agg_ready, r + 1)

                        def finish0():
                            if b:
                                dense_layer(r, w0).then_inc(dense_done, 1)
                            else:
                                with pe.If(a > 0):
                                    dense_layer(r, w0).then_inc(dense_done, 1)

                        multiply(n, c, acc[:, b, :], x_hi, x_lo, first, None if first else c < a,
                                 between=finish0 if first else None)
            dense_layer(NROW, w0).then_inc(dense_done, 1)

            def finish2(count):
                row_sums(count)
                dense_layer(count, w1).then_inc(dense_done, 1)

            def block2(a, b, second):
                before = a * 4 + (NROW + 2 * b + second)

                def finish():
                    if b or second:
                        finish2(before)
                    else:
                        with pe.If(a > 0):
                            finish2(before)

                def superblock(c):
                    pe.wait_ge(row_out, min(2 * c + 3, NROW + 1))

                    def between():
                        if c == (NSB - 1 if second else 0):
                            finish()
                        elif not second and c < NROW // 4:
                            with pe.If(a > c - 1):
                                finish()

                    end = second and b and c == NSB - NROW // 4
                    multiply(at2(a, b, second, c), c, acc[:, second, :], z_hi, z_lo, False,
                             ahead_if=(a < NROW // 4 - 1) if end else None, between=between)

                pe.wait_ge(agg_ready, before + 1)
                nc.tensor.matmul(acc[:, second, :], zeros[:, 0:P], zeros[:, :], start=True, stop=True)
                for c in reversed(range(NSB)) if second else range(NSB):
                    if (c == NSB - 1) if second else (c >= NROW // 4 - 1):
                        superblock(c)
                    elif second and c < NSB - NROW // 4:
                        continue
                    else:
                        with pe.If(c + a > NSB - 2 if second else a < c + 1):
                            superblock(c)

            with pe.Fori(0, NROW // 4) as a:
                for b in range(2):
                    for second in (0, 1):
                        block2(a, b, second)
            finish2(2 * NROW)

        @block.scalar
        def _(act):
            for t in range(TILES):
                act.dma_start(w_in[t::XT, :], w_quarter[t, 0::2]).then_inc(w_loaded, 16)
                act.dma_start(w_in[TILES + t::XT, :], w_rows[t, 1::2]).then_inc(w_loaded, 16)
            act.dma_start(w0[:, :], w_agg).then_inc(weights_loaded, 16)
            act.dma_start(w1[:, :], weight).then_inc(weights_loaded, 16)
            act.dma_start(w1_row[:, :], weight[D - 1:D, :].to_broadcast([P, D])
                          ).then_inc(weights_loaded, 16)
            act.wait_ge(w_turned, 1)
            nc.scalar.activation(exp_w[:, :], w_cols, ACT.Exp, scale=-1.0).then_inc(exp_done, 1)

            def high_p(n, j):
                act.wait_ge(p_turned, n * TILES + (j + 1 + TILES))
                act.wait_ge(p_mul, n * TILES + (j + 1))
                nc.scalar.activation(a_hi[:, TILES + j], turned_p[:, j % PSLOTS], ACT.Copy
                                     ).then_inc(p_hi, 1)

            def high_d(n, h):
                act.wait_ge(d_turned, n * 2 + (h + 3))
                act.wait_ge(d_mul, n * 2 + (h + 1))
                nc.scalar.activation(a_hi[:, 0:TILES, h * HALF:(h + 1) * HALF], turned_d[:, :, :],
                                     ACT.Copy).then_inc(d_hi, 1)

            def high(n, h):
                high_p(n, 2 * h)
                high_p(n, 2 * h + 1)
                high_d(n, h)

            def aggregate(nxt, b):
                act.wait_ge(d_mul, multiplied_before(nxt * NSB))
                nc.scalar.activation(by_tile(agg[:, :], b, True), by_tile(acc[:, b, :], b), ACT.Copy
                                     ).then_inc(agg_ready, 1)

            def relu0(nxt):
                act.wait_ge(dense_done, nxt)
                act.wait_ge(act_read, nxt)
                act.wait_ge(gate_step, 3)
                for s in range(SUB):
                    last = nc.scalar.activation(act_out[:, s, :], dense[:, s, :], ACT.Relu,
                                                scale=gate[:, bass.ds(nxt * SUB + s, 1)])
                last.then_inc(act_done, 1)

            def relu1(n2):
                act.wait_ge(dense_done, n2 + NROW)
                act.wait_ge(inv_done, n2)
                act.wait_ge(act_read, n2 + NROW)
                for s in range(SUB):
                    last = nc.scalar.activation(act_out[:, s, :], dense[:, s, :], ACT.Relu,
                                                scale=inv_sum[:, s:s + 1])
                last.then_inc(act_done, 1)

            with act.Fori(0, NROW // 2) as a:
                for b in range(2):
                    r = a * 2 + b
                    high(r * NSB, 0)
                    if b:
                        aggregate(r, 0)
                    else:
                        with act.If(a > 0):
                            aggregate(r, 1)
                    high(r * NSB, 1)
                    if b:
                        relu0(r)
                    else:
                        with act.If(a > 0):
                            relu0(r)
                    with act.Fori(1, NSB) as k:
                        for h in range(2):
                            high(r * NSB + k, h)
            aggregate(NROW, 1)
            relu0(NROW)
            with act.Fori(0, NROW // 4) as a:
                for b in range(2):
                    for second in (0, 1):
                        before = a * 4 + (2 * b + second)
                        left = a + 1 if second else NSB - a
                        with act.Fori(0, left) as j:
                            for h in range(2):
                                high(start2(a, b, second) + j, h)
                            with act.If(j < 1):
                                if b or second:
                                    relu1(before)
                                else:
                                    with act.If(a > 0):
                                        relu1(before)
            relu1(NROW)

        @block.vector
        def _(dve):
            nc.vector.memset(zeros[:, :].bitcast(F32), 0.0).then_inc(zeros_ready, 1)
            dve.wait_ge(exp_done, 1)
            nc.vector.tensor_scalar(exp_w[:, :], exp_w[:, :], 1.0, None, ALU.add).then_inc(gate_step, 1)
            dve.wait_ge(gate_step, 1)
            nc.vector.reciprocal(gate[:, SUB:], exp_w[:, :]).then_inc(gate_step, 1)
            dve.wait_ge(gate_step, 2)
            nc.vector.tensor_scalar(keep[:, :], gate[:, SUB:], -1.0, 2.0, ALU.mult, ALU.add
                                    ).then_inc(gate_step, 1)

            def low_p(n, j):
                dve.wait_ge(p_hi, n * TILES + (j + 1))
                nc.vector.tensor_tensor(a_lo[:, TILES + j], turned_p[:, j % PSLOTS],
                                        a_hi[:, TILES + j].bitcast(F32), ALU.subtract
                                        ).then_inc(p_lo, 1)

            def low(n, h):
                rows = slice(h * HALF, (h + 1) * HALF)
                dve.wait_ge(d_loaded[h], n * 64 + 64)
                dve.wait_ge(d_lo, n * 2 + h)
                nc.vector.transpose(
                    turned_d[:, :, :].rearrange("p t (g i) -> p t g i", g=GROUPS),
                    raw_d[:, h].rearrange("p g (t i) -> p t g i", t=TILES)).then_inc(d_turned, 1)
                low_p(n, 2 * h)
                low_p(n, 2 * h + 1)
                dve.wait_ge(d_hi, n * 2 + (h + 1))
                nc.vector.tensor_tensor(a_lo[:, 0:TILES, rows], turned_d[:, :, :],
                                        a_hi[:, 0:TILES, rows].bitcast(F32), ALU.subtract
                                        ).then_inc(d_lo, 1)

            def save_part(nxt):
                dve.wait_ge(d_mul, multiplied_before(nxt * NSB))
                dve.wait_ge(row_out, nxt)
                nc.vector.tensor_copy(part_out[:, :], acc_z[:, :]).then_inc(part_ready, 1)

            with dve.Fori(0, NROW // 2) as a:
                for b in range(2):
                    r = a * 2 + b
                    low(r * NSB, 0)
                    if b:
                        save_part(r)
                    else:
                        with dve.If(a > 0):
                            save_part(r)
                    low(r * NSB, 1)
                    with dve.Fori(1, NSB) as k:
                        for h in range(2):
                            low(r * NSB + k, h)
            save_part(NROW)

            def aggregate(n2, nxt, which, odd):
                dve.wait_ge(d_mul, multiplied_before(nxt))
                dve.wait_ge(part_loaded, n2 * 16)
                nc.vector.tensor_tensor(by_tile(agg[:, :], odd, True), by_tile(acc[:, which, :], odd),
                                        by_tile(part_in[:, :], odd),
                                        ALU.add).then_inc(agg_ready, 1)

            def inverse(n2):
                dve.wait_ge(dense_done, n2 + NROW)
                nc.vector.reciprocal(inv_sum[:, :], sums).then_inc(inv_done, 1)

            with dve.Fori(0, NROW // 4) as a:
                for b in range(2):
                    for second in (0, 1):
                        before = a * 4 + (2 * b + second)
                        left = a + 1 if second else NSB - a
                        begin = start2(a, b, second)

                        def previous(what, *args):
                            if b or second:
                                what(*args)
                            else:
                                with dve.If(a > 0):
                                    what(*args)

                        with dve.Fori(0, left) as j:
                            low(begin + j, 0)
                            with dve.If(j < 1):
                                previous(aggregate, before, begin, 1 - second,
                                         b)
                            low(begin + j, 1)
                            with dve.If(j < 1):
                                previous(inverse, before)
            aggregate(NROW, n_pass1 + NROW // 2 * (NSB + 1), 1, 0)
            inverse(NROW)

        @block.gpsimd
        def _(pool):
            g = nc.gpsimd
            g.memset(ident[:, :], 0.0).then_inc(pool_step, 1)
            pool.wait_ge(pool_step, 1)
            g.affine_select(out=ident[:, :], in_=ident[:, :], compare_op=ALU.not_equal, fill=1.0,
                            base=0, pattern=[[-1, P]], channel_multiplier=1).then_inc(ident_ready, 1)
            g.memset(minus_half[:, :], -0.5).then_inc(pool_step, 1)

            def load_x(k):
                r = 2 * (NSB - 1 - k)
                for q in range(4):
                    pool.dma_start(x_in[q * Q:(q + 1) * Q, k % 2, 0:TILES], x_quarter[r, q]
                                   ).then_inc(x_loaded[k % 2], 16)
                pool.dma_start(x_in[:, k % 2, TILES:XT], x_rows[r + 1]).then_inc(x_loaded[k % 2], 16)

            load_x(0)
            load_x(1)
            for k in range(NSB):
                tiles = slice((NSB - 1 - k) * XT, (NSB - k) * XT)
                pool.wait_ge(x_loaded[k % 2], 80 * (k // 2) + 80)
                g.tensor_copy(x_hi[:, tiles, :], x_in[:, k % 2]).then_inc(pool_step, 1)
                pool.wait_ge(pool_step, 3 + k)
                g.tensor_tensor(x_lo[:, tiles, :], x_in[:, k % 2], x_hi[:, tiles, :].bitcast(F32),
                                ALU.subtract).then_inc(x_ready, 1)
                if k + 2 < NSB:
                    pool.wait_ge(x_ready, k + 1)
                    load_x(k + 2)
            pool.wait_ge(weights_loaded, 48)
            g.tensor_tensor(w1[:, :], w1[:, :], w1_row[:, :], ALU.subtract).then_inc(pool_step, 1)
            pool.wait_ge(gate_step, 3)
            pool.wait_ge(pool_step, NSB + 3)

            def wide(ap):
                return ap.unsqueeze(2).to_broadcast([P, SUB, D])

            def row_sum(step, dst, src):
                half = D // 2
                step(g.tensor_tensor(fold[:, :, 0:half], src[:, :, 0:half], src[:, :, half:D], ALU.add))
                while half > 2:
                    half //= 2
                    step(g.tensor_tensor(fold[:, :, 0:half], fold[:, :, 0:half],
                                         fold[:, :, half:2 * half], ALU.add))
                step(g.tensor_tensor(dst, fold[:, :, 0], fold[:, :, 1], ALU.add))

            def norm(step, dst):
                row_sum(step, mean[:, :], v)
                step(g.tensor_scalar(mean[:, :], mean[:, :], 1.0 / D, None, ALU.mult))
                step(g.tensor_tensor(v[:, :, :], v[:, :, :], wide(mean[:, :]), ALU.subtract))
                step(g.tensor_tensor(sq[:, :, :], v[:, :, :], v[:, :, :], ALU.mult))
                row_sum(step, var[:, :], sq)
                step(g.tensor_scalar(var[:, :], var[:, :], 1.0 / D, LN_EPS, ALU.mult, ALU.add))
                step(g.tensor_tensor(rstd[:, :], var[:, :], minus_half[:, :], ALU.pow))
                return g.tensor_tensor(dst, v[:, :, :], wide(rstd[:, :]), ALU.mult)

            def counter():
                pool.sem_clear(pool_step)
                count = [0]

                def step(ins):
                    count[0] += 1
                    ins.then_inc(pool_step, 1)
                    pool.wait_ge(pool_step, count[0])
                return step, count

            with pool.Fori(0, NROW) as r:
                step, count = counter()
                tiles = bass.ds(r * SUB, SUB)
                pool.wait_ge(part_ready, r + 1)
                pool.dma_start(partial[r], part_out[:, :]).then_inc(part_stored, 16)
                step(g.tensor_tensor(v[:, :, :], x_hi[:, tiles, :].bitcast(F32),
                                     x_lo[:, tiles, :].bitcast(F32), ALU.add))
                step(g.tensor_tensor(v[:, :, :], v[:, :, :], wide(keep[:, tiles]), ALU.mult))
                pool.wait_ge(act_done, r + 2)
                step(g.tensor_tensor(v[:, :, :], v[:, :, :], act_out[:, :, :], ALU.add))
                pool.sem_inc(act_read, 1)
                step(norm(step, y[:, :, :]))
                step(g.tensor_copy(x1_last[:, tiles], y[:, :, D - 1]))
                step(g.memset(y[:, :, D - 1:D], 1.0))
                step(g.tensor_copy(z_hi[:, tiles, :], y[:, :, :]))
                pool.wait_ge(part_stored, r * 16 + 16)
                g.tensor_tensor(z_lo[:, tiles, :], y[:, :, :], z_hi[:, tiles, :].bitcast(F32),
                                ALU.subtract).then_inc(row_out, 1)

            pool.wait_ge(part_stored, NROW * 16)
            with pool.Fori(0, NROW // 4) as a:
                for b in range(2):
                    for second in (0, 1):
                        g2 = a * 4 + (2 * b + second)
                        r = a * -2 + (NROW - 1 - b) if second else a * 2 + b
                        tiles = bass.ds(r * SUB, SUB)
                        step, count = counter()
                        pool.wait_ge(agg_ready, g2 + (NROW + 2))
                        step(g.tensor_tensor(v[:, :, :], z_hi[:, tiles, :].bitcast(F32),
                                             z_lo[:, tiles, :].bitcast(F32), ALU.add))
                        pool.dma_start(part_in[:, :], partial[r]).then_inc(part_loaded, 16)
                        step(g.tensor_copy(v[:, :, D - 1], x1_last[:, tiles]))
                        pool.wait_ge(act_done, g2 + (NROW + 2))
                        step(g.tensor_scalar(sq[:, :, :], act_out[:, :, :], OUT_EPS, None, ALU.add))
                        pool.sem_inc(act_read, 1)
                        step(g.tensor_tensor(v[:, :, :], v[:, :, :], sq[:, :, :], ALU.add))
                        pool.wait_ge(y_stored, a * 160 + (0, 64, 80, 96)[2 * b + second])
                        step(norm(step, y[:, :, :]))
                        if (second + b) % 2:
                            pool.dma_start(out_rows[r], y[:, :, :]).then_inc(y_stored, 16)
                        else:
                            for q in range(4):
                                pool.dma_start(out_quarter[r, q], y[q * Q:(q + 1) * Q]
                                               ).then_inc(y_stored, 16)
            pool.wait_ge(y_stored, NROW // 4 * 160)


_INS = ["x", "adj", "L0_gnn_w", "L0_gnn_W_agg", "L1_gnn_weight"]


def kernel(**inputs):
    import concourse.bacc as bacc
    from concourse.bass_utils import run_bass_kernel_spmd

    nc = bacc.Bacc("TRN2", target_bir_lowering=False, num_devices=1)
    arrays, args = {}, []
    for name in _INS:
        a = np.ascontiguousarray(inputs[name])
        arrays[name] = a
        args.append(nc.dram_tensor(name, a.shape, mybir.dt.from_np(a.dtype), kind="ExternalInput").ap())
    out = nc.dram_tensor("y_out", (N, D), F32, kind="ExternalOutput").ap()
    build(nc, *args, out)
    return run_bass_kernel_spmd(nc, [arrays], core_ids=[0]).results[0]["y_out"]
```

```python
import numpy as np
import concourse.bass as bass
from concourse import mybir
from contextlib import ExitStack

F32 = mybir.dt.float32
F32R = mybir.dt.float32r
AX = mybir.AxisListType
ALU = mybir.AluOpType
ACT = mybir.ActivationFunctionType

P = 128
N = 8192
D = 128
ROWS = 512
SUB = ROWS // P
NROW = N // ROWS
TILES = ROWS // P
Q = P // 4
HALF = ROWS // 2
GROUPS = HALF // Q
SCOLS = 2 * ROWS
NSB = N // SCOLS
KT = N // P
XT = SCOLS // P
LAST_ROW = NROW // 2
LN_EPS = 1e-5
OUT_EPS = 1e-4


def build(nc, x, adj, w, w_agg, weight, out):
    assert NROW * ROWS == N and NSB * SCOLS == N and SCOLS == 2 * ROWS and NROW % 4 == 0
    n_pass1 = NROW * NSB
    partial = nc.dram_tensor("partial", (NROW, P, ROWS), F32, kind="Internal").ap()

    a_rows = adj.rearrange("(r s p) (c k) -> r c p s k", s=SUB // 2, p=P, k=ROWS)
    a_squares = adj.rearrange("(r g i) (q k) -> r q i g k", g=GROUPS, i=Q, k=P)
    x_in_order = x.rearrange("(c u p t) d -> c p u t d", u=2, t=TILES, p=P)
    out_in_order = out.rearrange("(r p t) d -> r p t d", t=TILES, p=P)
    w_in_order = w.rearrange("(r p t) -> p r t", t=TILES, p=P)

    with ExitStack() as ctx:
        def sb(name, shape, dt=F32):
            return ctx.enter_context(nc.sbuf_tensor(name, shape, dt))

        def ps(name, shape):
            return ctx.enter_context(nc.psum_tensor(name, shape, F32))

        def sem(name):
            return ctx.enter_context(nc.semaphore(name))

        x_hi = sb("x_hi", [P, KT, D], F32R)
        x_lo = sb("x_lo", [P, KT, D], F32R)
        z_hi = sb("z_hi", [P, KT, D], F32R)
        z_lo = sb("z_lo", [P, KT, D], F32R)
        x1_last = sb("x1_last", [P, KT])
        raw_p = sb("raw_p", [P, 2, HALF * ROWS // P])
        raw_d = sb("raw_d", [P, 2, HALF * ROWS // P])
        a_hi = sb("a_hi", [P, 2 * TILES, ROWS], F32R)
        a_lo = sb("a_lo", [P, 2 * TILES, ROWS], F32R)
        ident = sb("ident", [P, P])
        zeros = sb("zeros", [P, ROWS], F32R)
        w0 = sb("w0", [P, D])
        w1 = sb("w1", [P, D])
        w1_row = sb("w1_row", [P, D])
        w_in = sb("w_in", [P, NROW, TILES])
        exp_w = sb("exp_w", [P, KT])
        gate = sb("gate", [P, SUB + KT])
        keep = sb("keep", [P, KT])
        minus_half = sb("minus_half", [P, SUB])
        out_eps = sb("out_eps", [P, 1])
        x_in = sb("x_in", [P, 2, XT, D])
        agg = sb("agg", [P, ROWS])
        part_out = sb("part_out", [P, ROWS])
        part_in = sb("part_in", [P, 2, ROWS])
        act_out = sb("act_out", [P, 2, SUB, D])
        inv_sum = sb("inv_sum", [P, SUB])
        v = sb("v", [P, SUB, D])
        sq = sb("sq", [P, SUB, D])
        y = sb("y", [P, SUB, D])
        mean = sb("mean", [P, SUB])
        var = sb("var", [P, SUB])
        rstd = sb("rstd", [P, SUB])

        turned_p = ps("turned_p", [P, TILES, HALF])
        turned_d = ps("turned_d", [P, TILES, HALF])
        acc = ps("acc", [P, 2, ROWS])
        acc_z = ps("acc_z", [P, ROWS])
        sums = acc_z[:, 0:SUB]
        dense = ps("dense", [P, SUB, D])

        p_loaded = [sem(f"p_loaded{h}") for h in range(2)]
        d_loaded = [sem(f"d_loaded{h}") for h in range(2)]
        p_turned = sem("p_turned")
        p_hi = sem("p_hi")
        p_lo = sem("p_lo")
        p_mul = sem("p_mul")
        d_turned = sem("d_turned")
        d_hi = sem("d_hi")
        d_lo = sem("d_lo")
        d_mul = sem("d_mul")
        x_loaded = [sem(f"x_loaded{v}") for v in range(2)]
        x_hi_ready = sem("x_hi_ready")
        x_ready = sem("x_ready")
        w_loaded = sem("w_loaded")
        weights_loaded = sem("weights_loaded")
        weights_ready = sem("weights_ready")
        ident_ready = sem("ident_ready")
        zeros_ready = sem("zeros_ready")
        exp_done = sem("exp_done")
        gate_step = sem("gate_step")
        pool_step = sem("pool_step")
        agg_ready = sem("agg_ready")
        part_ready = sem("part_ready")
        part_stored = sem("part_stored")
        part_loaded = [sem(f"part_loaded{v}") for v in range(2)]
        dense_done = sem("dense_done")
        inv_done = sem("inv_done")
        act_done = sem("act_done")
        act_read = sem("act_read")
        row_out = sem("row_out")
        y_stored = sem("y_stored")
        pool_through = sem("pool_through")
        dve_step = sem("dve_step")
        last_var = sem("last_var")
        last_rstd = sem("last_rstd")
        last_y = sem("last_y")
        last_stored = sem("last_stored")

        def at1(r, c):
            return r * NSB + (NSB - 1) - c

        def at2(a, b, second, c):
            if second:
                return start2(a, b, True) + (NSB - 1 - c)
            return a * (2 * (NSB + 1) - 1) + b * (NSB + 1) + c + n_pass1

        def start2(a, b, second):
            if second:
                return a * (2 * (NSB + 1) - 1) + b * (NSB + 1) + (n_pass1 + NSB)
            return a * (2 * (NSB + 1)) + b * (NSB + 1) + n_pass1

        def multiplied_before(n):
            return n * 2 + 2

        def wide(ap):
            return ap.unsqueeze(2).to_broadcast([P, SUB, D])

        def row_sum(g, step, dst, src):
            if g is nc.vector:
                return step(g.tensor_reduce(dst, src[:, :, :], AX.X, ALU.add))
            half = D // 2
            step(g.tensor_tensor(sq[:, :, 0:half], src[:, :, 0:half], src[:, :, half:D], ALU.add))
            while half > 2:
                half //= 2
                step(g.tensor_tensor(sq[:, :, 0:half], sq[:, :, 0:half],
                                     sq[:, :, half:2 * half], ALU.add))
            step(g.tensor_tensor(dst, sq[:, :, 0], sq[:, :, 1], ALU.add))

        def norm(g, step, dst, inv_root):
            row_sum(g, step, mean[:, :], v)
            step(g.tensor_scalar(mean[:, :], mean[:, :], 1.0 / D, None, ALU.mult))
            step(g.tensor_tensor(v[:, :, :], v[:, :, :], wide(mean[:, :]), ALU.subtract))
            step(g.tensor_tensor(sq[:, :, :], v[:, :, :], v[:, :, :], ALU.mult))
            row_sum(g, step, var[:, :], sq)
            step(g.tensor_scalar(var[:, :], var[:, :], 1.0 / D, LN_EPS, ALU.mult, ALU.add))
            inv_root(step)
            return g.tensor_tensor(dst, v[:, :, :], wide(rstd[:, :]), ALU.mult)

        def restore_x1(g, step, tiles):
            step(g.tensor_tensor(v[:, :, :], z_hi[:, tiles, :].bitcast(F32),
                                 z_lo[:, tiles, :].bitcast(F32), ALU.add))
            step(g.tensor_copy(v[:, :, D - 1], x1_last[:, tiles]))

        def add_relu1(g, step, which):
            step(g.tensor_tensor(sq[:, :, :], act_out[:, which], wide_eps, ALU.add))
            step(g.tensor_tensor(v[:, :, :], v[:, :, :], sq[:, :, :], ALU.add))

        wide_eps = out_eps[:, :].unsqueeze(2).to_broadcast([P, SUB, D])

        block = ctx.enter_context(nc.Block())

        @block.sync
        def _(sp):
            def load_squares(dst, loaded, row, q0):
                for q in range(4):
                    sp.dma_start(dst[q * Q:(q + 1) * Q, :].rearrange("p (g k) -> p g k", k=P),
                                 a_squares[row, q0 + q]).then_inc(loaded, 16)

            def load_p(n, h, r, c):
                sp.dma_start(raw_p[:, h].rearrange("p (s k) -> p s k", k=ROWS),
                             a_rows[r * 2 + h, c * 2 + 1]).then_inc(p_loaded[h], 16)
                sp.sem_inc(p_loaded[h], 48)

            def load(n, r, c, pe_turns=(True, True)):
                for h in range(2):
                    sp.wait_ge(p_turned, n * 2 + (h + 1))
                    if pe_turns[h]:
                        load_p(n, h, r, c)
                    else:
                        load_squares(raw_p[:, h], p_loaded[h], r * 2 + h, c * XT + TILES)
                    sp.wait_ge(d_turned, n * 2 + (h + 1))
                    load_squares(raw_d[:, h], d_loaded[h], r * 2 + h, c * XT)

            with sp.Fori(0, NROW // 2) as a:
                for b in range(2):
                    with sp.Fori(0, NSB) as k:
                        def load1(pe_turns):
                            load((a * 2 + b) * NSB + k, a * 2 + b, k * -1 + (NSB - 1), pe_turns)

                        with sp.If(k + a < NSB):
                            load1((True, True))
                        with sp.If(k + a > NSB - 1):
                            with sp.If(k + a < NSB + 1):
                                load1((True, False))
                            with sp.If(k + a > NSB):
                                load1((False, False))
            with sp.Fori(0, NROW // 4) as a:
                for b in range(2):
                    with sp.Fori(a, NSB) as c:
                        load(at2(a, b, False, c), a * 2 + b, c)
                    with sp.Fori(0, a + 1) as j:
                        load(start2(a, b, True) + j, a * -2 + (NROW - 1 - b), j * -1 + (NSB - 1))
            sp.wait_ge(last_y, 1)
            sp.dma_start(out_in_order[LAST_ROW], y[:, :, :]).then_inc(last_stored, 16)
            sp.wait_ge(last_stored, 16)

        @block.tensor
        def _(pe):
            def turn(n, h):
                pe.wait_ge(p_loaded[h], n * 64 + 64)
                for t in range(TILES):
                    for s in range(HALF // P):
                        last = nc.tensor.transpose(
                            turned_p[:, t, s * P:(s + 1) * P],
                            raw_p[:, h, s * ROWS + t:(s + 1) * ROWS:TILES], ident[:, :])
                last.then_inc(p_turned, 1)

            def product(dst, left, right):
                return nc.tensor.matmul(dst, left, right, start=False, stop=False,
                                        skip_group_check=True)

            def piece(dst, hi, lo, c, part, h):
                rows = slice(h * HALF, (h + 1) * HALF)
                for t in range(TILES):
                    stationary, turned = c * XT + part * TILES + t, part * TILES + t
                    product(dst[:, rows], lo[:, stationary, :], a_hi[:, turned, rows])
                    product(dst[:, rows], hi[:, stationary, :], a_hi[:, turned, rows])
                    last = product(dst[:, rows], hi[:, stationary, :], a_lo[:, turned, rows])
                return last

            def multiply(n, c, dst, hi, lo, next_if=True, z_rows=None, z_late=False, between=None):
                def wait_z():
                    pe.wait_ge(row_out, z_rows + 1)

                both = z_rows is not None
                for h in range(2):
                    pe.wait_ge(p_lo, n * 2 + (h + 3))
                    if h == 0:
                        if not both:
                            turn(n, 1)
                    elif next_if is True:
                        turn(n + 1, 0)
                    elif next_if is not False:
                        with pe.If(next_if):
                            turn(n + 1, 0)
                    last_p = piece(dst, hi, lo, c, 1, h)
                    if both and not z_late:
                        wait_z()
                        last_p = piece(acc_z, z_hi, z_lo, c, 1, h)
                    if not z_late:
                        last_p.then_inc(p_mul, 1)
                    pe.wait_ge(d_lo, n * 2 + (h + 3))
                    last_d = piece(dst, hi, lo, c, 0, h)
                    if z_late:
                        wait_z()
                        piece(acc_z, z_hi, z_lo, c, 1, h).then_inc(p_mul, 1)
                    if both:
                        last_d = piece(acc_z, z_hi, z_lo, c, 0, h)
                    last_d.then_inc(d_mul, 1)
                    if between and h == 0:
                        between()

            def dense_layer(count, weights):
                pe.wait_ge(agg_ready, count + 2)
                pe.wait_ge(act_done, count)
                pe.wait_ge(weights_ready, 1)
                for t in range(TILES):
                    last = nc.tensor.matmul(dense[:, t, :], agg_tile(t), weights[:, :],
                                            start=True, stop=True)
                return last

            def row_sums(count):
                pe.wait_ge(agg_ready, count + 2)
                pe.wait_ge(part_ready, NROW + 1)
                for t in range(TILES):
                    nc.tensor.matmul(sums[:, t:t + 1], agg_tile(t), ident[:, D - 1:D],
                                     start=True, stop=True)

            def agg_tile(t):
                return agg[:, t:ROWS:TILES]

            pe.sem_inc(p_turned, 2)
            pe.sem_inc(p_mul, 2)
            pe.sem_inc(p_lo, 2)
            pe.sem_inc(d_lo, 2)
            pe.sem_inc(part_ready, 1)
            pe.sem_inc(d_turned, 2)
            pe.sem_inc(d_mul, 2)
            pe.sem_inc(act_read, 2)
            pe.sem_inc(agg_ready, 2)
            pe.sem_inc(act_done, 1)
            pe.sem_inc(row_out, 1)
            pe.wait_ge(ident_ready, 1)
            pe.wait_ge(zeros_ready, 1)
            turn(0, 0)

            with pe.Fori(0, NROW // 2) as a:
                for b in range(2):
                    r = a * 2 + b
                    for c in reversed(range(NSB)):
                        n = at1(r, c)
                        if c == NSB - 2:
                            pe.wait_ge(part_ready, r + 1)
                            nc.tensor.matmul(acc_z[:, :], zeros[:, 0:P], zeros[:, :],
                                             start=True, stop=True)
                        pe.wait_ge(x_ready, NSB - c)
                        if c == NSB - 1:
                            pe.wait_ge(agg_ready, r + 1)
                            nc.tensor.matmul(acc[:, b, :], zeros[:, 0:P], zeros[:, :],
                                             start=True, stop=True)

                            def finish0():
                                if b:
                                    dense_layer(r, w0).then_inc(dense_done, 1)
                                else:
                                    with pe.If(a > 0):
                                        dense_layer(r, w0).then_inc(dense_done, 1)

                            multiply(n, c, acc[:, b, :], x_hi, x_lo, between=finish0)
                            continue
                        with pe.If(a > c):
                            multiply(n, c, acc[:, b, :], x_hi, x_lo, next_if=c == 0,
                                     z_rows=2 * c + 2, z_late=not b and c >= NSB - 3)
                        with pe.If(a < c + 1):
                            multiply(n, c, acc[:, b, :], x_hi, x_lo)

            def finish2(count):
                row_sums(count)
                dense_layer(count, w1).then_inc(dense_done, 1)

            def block2(a, b, second):
                before = a * 4 + (NROW + 2 * b + second)

                def finish():
                    if b or second:
                        finish2(before)
                    else:
                        with pe.If(a > 0):
                            finish2(before)
                        with pe.If(a < 1):
                            dense_layer(NROW, w0).then_inc(dense_done, 1)

                def superblock(c):
                    pe.wait_ge(row_out, min(2 * c + 3, NROW + 1))

                    def between():
                        if c == (NSB - 1 if second else 0):
                            finish()
                        elif not second and c < NROW // 4:
                            with pe.If(a > c - 1):
                                finish()

                    end = second and b and c == NSB - NROW // 4
                    multiply(at2(a, b, second, c), c, acc[:, second, :], z_hi, z_lo,
                             next_if=(a < NROW // 4 - 1) if end else True, between=between)

                pe.wait_ge(agg_ready, before + 1)
                nc.tensor.matmul(acc[:, second, :], zeros[:, 0:P], zeros[:, :], start=True, stop=True)
                for c in reversed(range(NSB)) if second else range(NSB):
                    if (c == NSB - 1) if second else (c >= NROW // 4 - 1):
                        superblock(c)
                    elif second and c < NSB - NROW // 4:
                        continue
                    else:
                        with pe.If(c + a > NSB - 2 if second else a < c + 1):
                            superblock(c)

            with pe.Fori(0, NROW // 4) as a:
                for b in range(2):
                    for second in (0, 1):
                        block2(a, b, second)
            finish2(2 * NROW)

        @block.scalar
        def _(act):
            def load_x(k):
                act.dma_start(x_in[:, k % 2].rearrange("p (u t) d -> p u t d", u=2),
                              x_in_order[NSB - 1 - k]).then_inc(x_loaded[k % 2], 16)

            load_x(0)

            def high_x(k):
                act.wait_ge(x_loaded[k % 2], 16 * (k // 2 + 1))
                nc.scalar.activation(x_hi[:, (NSB - 1 - k) * XT:(NSB - k) * XT, :], x_in[:, k % 2],
                                     ACT.Copy).then_inc(x_hi_ready, 1)

            def high(n, h):
                rows = slice(h * HALF, (h + 1) * HALF)
                act.wait_ge(p_turned, n * 2 + (h + 3))
                act.wait_ge(p_mul, n * 2 + (h + 1))
                nc.scalar.activation(a_hi[:, TILES:, rows], turned_p[:, :, :], ACT.Copy
                                     ).then_inc(p_hi, 1)
                act.wait_ge(d_turned, n * 2 + (h + 3))
                act.wait_ge(d_mul, n * 2 + (h + 1))
                nc.scalar.activation(a_hi[:, 0:TILES, rows], turned_d[:, :, :], ACT.Copy
                                     ).then_inc(d_hi, 1)

            def aggregate(nxt, b):
                act.wait_ge(d_mul, multiplied_before(nxt * NSB))
                nc.scalar.activation(agg[:, :], acc[:, b, :], ACT.Copy).then_inc(agg_ready, 1)
                act.wait_ge(row_out, nxt)
                nc.scalar.activation(part_out[:, :], acc_z[:, :], ACT.Copy).then_inc(part_ready, 1)

            def relu0(nxt, b):
                act.wait_ge(dense_done, nxt)
                act.wait_ge(act_read, nxt)
                act.wait_ge(gate_step, 3)
                for s in range(SUB):
                    last = nc.scalar.activation(act_out[:, b, s, :], dense[:, s, :], ACT.Relu,
                                                scale=gate[:, bass.ds(nxt * SUB + s, 1)])
                last.then_inc(act_done, 1)

            def relu1(n2, second):
                act.wait_ge(dense_done, n2 + NROW)
                act.wait_ge(inv_done, n2)
                act.wait_ge(act_read, n2 + NROW)
                for s in range(SUB):
                    last = nc.scalar.activation(act_out[:, second, s, :], dense[:, s, :], ACT.Relu,
                                                scale=inv_sum[:, s:s + 1])
                last.then_inc(act_done, 1)

            def first_row_block():
                high_x(0)
                load_x(1)
                act.dma_start(w_in[:, :, :], w_in_order).then_inc(w_loaded, 16)
                act.dma_start(w0[:, :], w_agg).then_inc(weights_loaded, 16)
                act.dma_start(w1[:, :], weight).then_inc(weights_loaded, 16)
                act.dma_start(w1_row[:, :], weight[D - 1:D, :].to_broadcast([P, D])
                              ).then_inc(weights_loaded, 16)
                for k in range(NSB):
                    high(k, 0)
                    if k + 1 < NSB:
                        high_x(k + 1)
                    high(k, 1)
                    if k + 2 < NSB:
                        act.wait_ge(x_ready, k + 1)
                        load_x(k + 2)
                act.wait_ge(w_loaded, 16)
                nc.scalar.activation(exp_w[:, :], w_in[:, :, :].rearrange("p r t -> p (r t)"),
                                     ACT.Exp, scale=-1.0).then_inc(exp_done, 1)

            def row_block(r, b):
                high(r * NSB, 0)
                aggregate(r, 1 - b)
                high(r * NSB, 1)
                relu0(r, 1 - b)
                with act.Fori(1, NSB) as k:
                    for h in range(2):
                        high(r * NSB + k, h)

            first_row_block()
            row_block(1, 1)
            with act.Fori(1, NROW // 2) as a:
                for b in range(2):
                    row_block(a * 2 + b, b)
            with act.Fori(0, NROW // 4) as a:
                for b in range(2):
                    for second in (0, 1):
                        before = a * 4 + (2 * b + second)
                        left = a + 1 if second else NSB - a
                        with act.Fori(0, left) as j:
                            high(start2(a, b, second) + j, 0)
                            if not b and not second:
                                with act.If(a * NSB + j < 1):
                                    aggregate(NROW, 1)
                            high(start2(a, b, second) + j, 1)
                            with act.If(j < 1):
                                if b or second:
                                    relu1(before, 1 - second)
                                else:
                                    with act.If(a > 0):
                                        relu1(before, 1)
                                    with act.If(a < 1):
                                        relu0(NROW, 1)
            relu1(NROW, 1)

        @block.vector
        def _(dve):
            nc.vector.memset(zeros[:, :].bitcast(F32), 0.0).then_inc(zeros_ready, 1)

            def gates():
                dve.wait_ge(exp_done, 1)
                nc.vector.tensor_scalar(exp_w[:, :], exp_w[:, :], 1.0, None, ALU.add
                                        ).then_inc(gate_step, 1)
                dve.wait_ge(gate_step, 1)
                nc.vector.reciprocal(gate[:, SUB:], exp_w[:, :]).then_inc(gate_step, 1)
                dve.wait_ge(gate_step, 2)
                nc.vector.tensor_scalar(keep[:, :], gate[:, SUB:], -1.0, 2.0, ALU.mult, ALU.add
                                        ).then_inc(gate_step, 1)

            def turn(turned, raw):
                return nc.vector.transpose(
                    turned[:, :, :].rearrange("p t (g i) -> p t g i", g=GROUPS),
                    raw.rearrange("p (g i t) -> p t g i", g=GROUPS, t=TILES))

            def low(n, h, next_if=None):
                rows = slice(h * HALF, (h + 1) * HALF)
                dve.wait_ge(d_loaded[h], n * 64 + 64)
                dve.wait_ge(d_lo, n * 2 + (h + 2))
                turn(turned_d, raw_d[:, h]).then_inc(d_turned, 1)
                dve.wait_ge(p_hi, n * 2 + (h + 1))
                nc.vector.tensor_tensor(a_lo[:, TILES:, rows], turned_p[:, :, :],
                                        a_hi[:, TILES:, rows].bitcast(F32), ALU.subtract
                                        ).then_inc(p_lo, 1)
                if next_if is not None:
                    with dve.If(next_if):
                        dve.wait_ge(p_loaded[1 - h], (n + h) * 64 + 64)
                        dve.wait_ge(p_lo, n * 2 + (h + 3))
                        turn(turned_p, raw_p[:, 1 - h]).then_inc(p_turned, 1)
                dve.wait_ge(d_hi, n * 2 + (h + 1))
                nc.vector.tensor_tensor(a_lo[:, 0:TILES, rows], turned_d[:, :, :],
                                        a_hi[:, 0:TILES, rows].bitcast(F32), ALU.subtract
                                        ).then_inc(d_lo, 1)

            with dve.Fori(0, NROW // 2) as a:
                for b in range(2):
                    r = a * 2 + b
                    with dve.Fori(0, NSB - 1) as k:
                        for h in range(2):
                            low(r * NSB + k, h, k + a > NSB - 1)
                    low(r * NSB + (NSB - 1), 0, a > 0)
                    low(r * NSB + (NSB - 1), 1)
                    if not b:
                        with dve.If(a < 1):
                            gates()

            def aggregate(count, nxt, which):
                dve.wait_ge(d_mul, multiplied_before(nxt))
                dve.wait_ge(part_loaded[which], count)
                nc.vector.tensor_tensor(agg[:, :], acc[:, which, :], part_in[:, which, :], ALU.add
                                        ).then_inc(agg_ready, 1)

            def inverse(n2):
                dve.wait_ge(dense_done, n2 + NROW)
                nc.vector.reciprocal(inv_sum[:, :], sums).then_inc(inv_done, 1)

            with dve.Fori(0, NROW // 4) as a:
                for b in range(2):
                    for second in (0, 1):
                        before = a * 4 + (2 * b + second)
                        left = a + 1 if second else NSB - a
                        begin = start2(a, b, second)

                        def previous(what, *args):
                            if b or second:
                                what(*args)
                            else:
                                with dve.If(a > 0):
                                    what(*args)

                        with dve.Fori(0, left) as j:
                            low(begin + j, 0)
                            with dve.If(j < 1):
                                previous(aggregate, a * 32 + 16 * (b + second), begin,
                                         1 - second)
                            low(begin + j, 1)
                            with dve.If(j < 1):
                                previous(inverse, before)
            aggregate(NROW * 8, n_pass1 + NROW // 2 * (NSB + 1), 1)
            inverse(NROW)

            count = [0]

            def step(ins):
                count[0] += 1
                ins.then_inc(dve_step, 1)
                dve.wait_ge(dve_step, count[0])
            tiles = slice(LAST_ROW * SUB, (LAST_ROW + 1) * SUB)
            dve.wait_ge(pool_through, 1)
            restore_x1(nc.vector, step, tiles)
            dve.wait_ge(act_done, 2 * NROW + 1)
            add_relu1(nc.vector, step, 1)

            def root_by_pool(step):
                dve.sem_inc(last_var, 1)
                dve.wait_ge(last_rstd, 1)
            norm(nc.vector, step, y[:, :, :], root_by_pool).then_inc(last_y, 1)

        @block.gpsimd
        def _(pool):
            g = nc.gpsimd
            g.memset(ident[:, :], 0.0).then_inc(pool_step, 1)
            pool.wait_ge(pool_step, 1)
            g.affine_select(out=ident[:, :], in_=ident[:, :], compare_op=ALU.not_equal, fill=1.0,
                            base=0, pattern=[[-1, P]], channel_multiplier=1).then_inc(ident_ready, 1)
            g.memset(minus_half[:, :], -0.5).then_inc(pool_step, 1)
            g.memset(out_eps[:, :], OUT_EPS).then_inc(pool_step, 1)

            for k in range(NSB):
                tiles = slice((NSB - 1 - k) * XT, (NSB - k) * XT)
                pool.wait_ge(x_hi_ready, k + 1)
                g.tensor_tensor(x_lo[:, tiles, :], x_in[:, k % 2], x_hi[:, tiles, :].bitcast(F32),
                                ALU.subtract).then_inc(x_ready, 1)
            pool.wait_ge(weights_loaded, 48)
            g.tensor_tensor(w1[:, :], w1[:, :], w1_row[:, :], ALU.subtract
                            ).then_inc(weights_ready, 1)
            pool.wait_ge(gate_step, 3)
            pool.wait_ge(pool_step, 3)

            def inv_root(step):
                step(g.tensor_tensor(rstd[:, :], var[:, :], minus_half[:, :], ALU.pow))

            def counter():
                pool.sem_clear(pool_step)
                count = [0]

                def step(ins):
                    count[0] += 1
                    ins.then_inc(pool_step, 1)
                    pool.wait_ge(pool_step, count[0])
                return step

            def row_block0(r, b):
                step = counter()
                tiles = bass.ds(r * SUB, SUB)
                pool.wait_ge(part_ready, r + 2)
                pool.dma_start(partial[r], part_out[:, :]).then_inc(part_stored, 16)
                step(g.tensor_tensor(v[:, :, :], x_hi[:, tiles, :].bitcast(F32),
                                     x_lo[:, tiles, :].bitcast(F32), ALU.add))
                step(g.tensor_tensor(v[:, :, :], v[:, :, :], wide(keep[:, tiles]), ALU.mult))
                pool.wait_ge(act_done, r + 2)
                step(g.tensor_tensor(v[:, :, :], v[:, :, :], act_out[:, b], ALU.add))
                pool.sem_inc(act_read, 1)
                step(norm(g, step, y[:, :, :], inv_root))
                step(g.tensor_copy(x1_last[:, tiles], y[:, :, D - 1]))
                step(g.memset(y[:, :, D - 1:D], 1.0))
                step(g.tensor_tensor(z_hi[:, tiles, :], y[:, :, :],
                                     zeros[:, :].bitcast(F32).rearrange("p (t d) -> p t d", t=SUB),
                                     ALU.add))
                pool.wait_ge(part_stored, r * 16 + 16)
                g.tensor_tensor(z_lo[:, tiles, :], y[:, :, :], z_hi[:, tiles, :].bitcast(F32),
                                ALU.subtract).then_inc(row_out, 1)

            pool.wait_ge(zeros_ready, 1)
            with pool.Fori(0, NROW // 2) as a:
                for b in range(2):
                    row_block0(a * 2 + b, b)

            def load_part(r, which):
                pool.dma_start(part_in[:, which, :], partial[r]).then_inc(part_loaded[which], 16)

            def row_block1(a, b, second):
                r = a * -2 + (NROW - 1 - b) if second else a * 2 + b
                step = counter()
                restore_x1(g, step, bass.ds(r * SUB, SUB))
                pool.wait_ge(act_done, a * 4 + (NROW + 2 + 2 * b + second))
                add_relu1(g, step, second)
                pool.sem_inc(act_read, 1)
                if b or second:
                    pool.wait_ge(y_stored, a * 64 + 16 * (2 * b + second))
                else:
                    with pool.If(a > 0):
                        pool.wait_ge(y_stored, a * 64)
                step(norm(g, step, y[:, :, :], inv_root))
                pool.dma_start(out_in_order[r], y[:, :, :]).then_inc(y_stored, 16)

            pool.wait_ge(part_stored, NROW * 16)
            load_part(0, 0)
            load_part(NROW - 1, 1)
            with pool.Fori(0, NROW // 4) as a:
                for b in range(2):
                    for second in (0, 1):
                        pool.wait_ge(agg_ready, a * 4 + (NROW + 3 + 2 * b + second))
                        load_part(a * -2 + (NROW - 2 - b) if second else a * 2 + (b + 1), second)
                        if second and b:
                            with pool.If(a < NROW // 4 - 1):
                                row_block1(a, b, second)
                        else:
                            row_block1(a, b, second)
            pool.wait_ge(y_stored, 16 * (NROW - 1))
            pool.sem_inc(pool_through, 1)
            pool.wait_ge(last_var, 1)
            g.tensor_tensor(rstd[:, :], var[:, :], minus_half[:, :], ALU.pow).then_inc(last_rstd, 1)
            for loaded in part_loaded:
                pool.wait_ge(loaded, (NROW // 2 + 1) * 16)


_INS = ["x", "adj", "L0_gnn_w", "L0_gnn_W_agg", "L1_gnn_weight"]


def kernel(**inputs):
    import concourse.bacc as bacc
    from concourse.bass_utils import run_bass_kernel_spmd

    nc = bacc.Bacc("TRN2", target_bir_lowering=False, num_devices=1)
    arrays, args = {}, []
    for name in _INS:
        a = np.ascontiguousarray(inputs[name])
        arrays[name] = a
        args.append(nc.dram_tensor(name, a.shape, mybir.dt.from_np(a.dtype), kind="ExternalInput").ap())
    out = nc.dram_tensor("y_out", (N, D), F32, kind="ExternalOutput").ap()
    build(nc, *args, out)
    return run_bass_kernel_spmd(nc, [arrays], core_ids=[0]).results[0]["y_out"]
```
